# Optimizing a Trainium2 kernel written in Bass

```python
import numpy as np
import jax
import jax.numpy as jnp

def _softmax(x, axis=-1):
    return jax.nn.softmax(x, axis=axis)
def _gelu(x):
    return jax.nn.gelu(x, approximate=True)
def _silu(x):
    return jax.nn.silu(x)
def _sigmoid(x):
    return jax.nn.sigmoid(x)
def _layernorm(x, axis=-1, eps=1e-5):
    m = jnp.mean(x, axis=axis, keepdims=True)
    v = jnp.var(x, axis=axis, keepdims=True)
    return (x - m) / jnp.sqrt(v + eps)
def _scatter_add(tgt, idx, src, axis=0):
    return tgt.at[idx].add(src)
def _segment_sum(src, seg, n):
    return jax.ops.segment_sum(src, seg, n)

kernel_name = 'mk_conv_preact_d1_conv_nchw256_e9570a'

def setup_inputs(seed: int = 0):
    np.random.seed(seed)
    _w = jnp.asarray
    def _rec_inputs():
        import jax
        import jax.numpy as jnp
        _gk = jax.random.key(seed)
        x = -7.109e-05 + 0.9999 * jax.random.normal(jax.random.fold_in(_gk, 1), (16, 256, 128, 128), jnp.float32)
        return x
    x = _rec_inputs()
    def _L0_conv_setup():
        import jax, jax.numpy as jnp
        import numpy as np
        POS_IDX = np.array([0, 2, 4, 10, 14, 20, 22, 24])
        NEG_IDX = np.array([6, 7, 8, 11, 13, 16, 17, 18])

        def _build_rpdc_kernel(weight):
            C = weight.shape[0]
            w = weight.reshape(C, 1, 9)
            tap = w[:, :, 1:]
            buf = jnp.zeros((C, 1, 25), dtype=weight.dtype)
            buf = buf.at[:, :, POS_IDX].set(tap)
            buf = buf.at[:, :, NEG_IDX].set(-tap)
            return buf.reshape(C, 1, 5, 5)
        key = jax.random.key(seed)
        kx, kw = jax.random.split(key)
        x = jax.random.normal(kx, (16, 256, 128, 128), dtype=jnp.float32)
        weight = jax.random.normal(kw, (256, 1, 3, 3), dtype=jnp.float32) * 0.1
        return {'x': x, 'weight': weight}
    _L0_conv_all = _L0_conv_setup()
    _L0_conv_in = {k: v for k, v in _L0_conv_all.items() if k in ('weight', )}
    del _L0_conv_all

    return {
        "x": x,
        "L0_conv_weight": _L0_conv_in["weight"],
    }

def reference(x, L0_conv_weight):
    import jax
    import jax.numpy as jnp
    def _L0_conv_ref(x, weight):
        import jax, jax.numpy as jnp
        import numpy as np
        POS_IDX = np.array([0, 2, 4, 10, 14, 20, 22, 24])
        NEG_IDX = np.array([6, 7, 8, 11, 13, 16, 17, 18])

        def _build_rpdc_kernel(weight):
            C = weight.shape[0]
            w = weight.reshape(C, 1, 9)
            tap = w[:, :, 1:]
            buf = jnp.zeros((C, 1, 25), dtype=weight.dtype)
            buf = buf.at[:, :, POS_IDX].set(tap)
            buf = buf.at[:, :, NEG_IDX].set(-tap)
            return buf.reshape(C, 1, 5, 5)
        C = weight.shape[0]
        kernel = _build_rpdc_kernel(weight)
        return jax.lax.conv_general_dilated(x, kernel, window_strides=(1, 1), padding=[(2, 2), (2, 2)], rhs_dilation=(1, 1), dimension_numbers=('NCHW', 'OIHW', 'NCHW'), feature_group_count=C)

    def _gn(v, G=32, eps=1e-5):
        B_, C_, H_, W_ = v.shape
        g = v.reshape(B_, G, C_ // G, H_, W_)
        m = jnp.mean(g, axis=(2, 3, 4), keepdims=True)
        s = jnp.var(g, axis=(2, 3, 4), keepdims=True)
        return ((g - m) / jnp.sqrt(s + eps)).reshape(v.shape)

    def _ln_c(v, eps=1e-6):
        m = jnp.mean(v, axis=1, keepdims=True)
        s = jnp.var(v, axis=1, keepdims=True)
        return (v - m) / jnp.sqrt(s + eps)

    def _ln_t(v, eps=1e-5):
        m = jnp.mean(v, axis=-1, keepdims=True)
        s = jnp.var(v, axis=-1, keepdims=True)
        return (v - m) / jnp.sqrt(s + eps)

    def _to_tokens(v):
        B_, C_, H_, W_ = v.shape
        return v.reshape(B_, C_, H_ * W_).transpose(0, 2, 1)
    def _from_tokens(t, like):
        B_, C_, H_, W_ = like.shape
        return t.transpose(0, 2, 1).reshape(B_, C_, H_, W_)

    x = x + _L0_conv_ref(_gn(x), L0_conv_weight)
    return x


_drawn_inputs = setup_inputs


def setup_inputs(seed=0):
    import zlib

    import numpy as np

    out = dict(_drawn_inputs(seed))
    spreads = {}
    factors = {}
    for name, (base, spread) in spreads.items():
        noise = np.random.default_rng([zlib.crc32(name.encode()), seed]).standard_normal(out[name].shape)
        drawn = base * np.exp(spread * noise) if base else spread * noise
        out[name] = jnp.asarray(drawn.astype(out[name].dtype))
    for name, factor in factors.items():
        out[name] = (out[name] * factor).astype(out[name].dtype)
    return out
```

```python
from contextlib import ExitStack

import numpy as np

import concourse.bass as bass
from concourse import mybir

F32 = mybir.dt.float32
F32R = mybir.dt.float32r
ALU = mybir.AluOpType
ACT = mybir.ActivationFunctionType
AX_X = mybir.AxisListType.X

P = 128
TAPS = 8
DX = 5
PERIOD = 5
CG = 8
QB = 4
SLOTS = 4
BANKS = 4
EPS = 1e-5

POS = [0, 2, 4, 10, 14, 20, 22, 24]
NEG = [6, 7, 8, 11, 13, 16, 17, 18]

STAT_STEPS = ["sum_means", "mean", "diff", "diff2", "m2", "sum_m2", "var", "inv", "inv2", "ratio", "corr",
              "scale", "shift"]


def after(t, step):
    return t * len(STAT_STEPS) + (STAT_STEPS.index(step) + 1)


def preact_conv(nc, x, taps, tap_select, band_mask, out):
    B, C, H, W = x.shape
    G = C // CG
    NQ = B // QB
    assert H == P and NQ == SLOTS
    BW = (P + PERIOD - 1) // PERIOD * PERIOD
    WP = W + DX - 1
    NJ = DX * PERIOD
    SUBS = 4
    SUB_COUNT = CG * W // SUBS
    N_MEANS = P * SUBS
    N_ALL = CG * H * W

    x_q = x.rearrange("(q b) (g c) h w -> g q b h c w", b=QB, c=CG)
    out_q = out.rearrange("(q b) (g c) h w -> g q b h c w", b=QB, c=CG)

    with ExitStack() as ctx:
        def sb(name, shape, dt=F32):
            return ctx.enter_context(nc.sbuf_tensor(name, shape, dt))

        def sem(name):
            return ctx.enter_context(nc.semaphore(name))

        xt = sb("xt", [P, SLOTS, QB, CG, W])
        hi = sb("hi", [P, 2, QB, CG, WP], F32R)
        lo = sb("lo", [P, 2, QB, CG, WP], F32R)
        xn = sb("xn", [P, 2, CG, W])
        bands = sb("bands", [P, CG, 2, DX, BW], F32R)
        periods = sb("periods", [P, C, NJ])
        per_hi = sb("per_hi", [P, CG, NJ], F32R)
        per_lo = sb("per_lo", [P, CG, NJ], F32R)
        mask = sb("mask", [P, BW])
        ones = sb("ones", [P, P])
        bn = sb("bn", [P, 2, QB, 2, 6])
        sum_means = sb("sum_means", [P, QB])
        mean = sb("mean", [P, QB])
        diff = sb("diff", [P, QB, SUBS])
        diff2 = sb("diff2", [P, QB, SUBS])
        m2 = sb("m2", [P, QB, SUBS])
        sum_m2 = sb("sum_m2", [P, QB])
        var = sb("var", [P, QB])
        root = sb("root", [P, QB])
        inv = sb("inv", [P, QB])
        inv2 = sb("inv2", [P, QB])
        ratio = sb("ratio", [P, QB])
        corr = sb("corr", [P, QB])
        scale = sb("scale", [P, 2, QB])
        shift = sb("shift", [P, 2, QB])
        scratch = xt[0:TAPS, SLOTS - 1].rearrange("p b c w -> p (b c w)")
        select_t = scratch[:, 0:NJ * P].rearrange("t (j k) -> t j k", j=NJ)
        taps_t = scratch[:, NJ * P:NJ * P + C]

        conv = ctx.enter_context(nc.psum_tensor("conv", [P, BANKS, QB * W], F32))
        sums = ctx.enter_context(nc.psum_tensor("sums", [P, 512], F32))
        sum_mean_ps = sums[:, 0:QB]
        sum_m2_ps = sums[:, 2 * QB:3 * QB]

        loaded = [sem(f"loaded{k}") for k in range(SLOTS)]
        stored = sem("stored")
        consts_in = sem("consts_in")
        ones_set = sem("ones_set")
        pads_set = sem("pads_set")
        period_made = sem("period_made")
        period_kept = sem("period_kept")
        period_split = sem("period_split")
        band_hi_made = sem("band_hi_made")
        band_lo_made = sem("band_lo_made")
        bn_done = sem("bn_done")
        stat_step = sem("stat_step")
        stat_sums = sem("stat_sums")
        root_done = sem("root_done")
        xn_made = sem("xn_made")
        hi_made = sem("hi_made")
        lo_made = sem("lo_made")
        conv_made = sem("conv_made")
        bank_free = sem("bank_free")

        block = ctx.enter_context(nc.Block())

        @block.sync
        def _(sp):
            def load(g, k):
                for b in range(QB):
                    sp.dma_start(xt[:, k, b], x_q[g, k, b]).then_inc(loaded[k], 16)

            sp.dma_start(select_t, tap_select).then_inc(consts_in, 16)
            sp.dma_start(taps_t, taps).then_inc(consts_in, 16)
            sp.dma_start(mask[:, :], band_mask).then_inc(consts_in, 16)
            for k in range(SLOTS):
                if k == SLOTS - 1:
                    sp.wait_ge(period_made, NJ)
                load(0, k)

            def store(g, k):
                t = g * SLOTS + k
                sp.wait_ge(bank_free, t * CG + CG + BANKS)
                for b in range(QB):
                    sp.dma_start(out_q[g, k, b], xt[:, k, b]).then_inc(stored, 16)
                sp.wait_ge(stored, (t * 16 + 16) * QB)

            with sp.Fori(0, G - 1) as g:
                for k in range(SLOTS):
                    store(g, k)
                    load(g + 1, k)
            for k in range(SLOTS):
                store(G - 1, k)

        @block.tensor
        def _(pe):
            pe.wait_ge(consts_in, 48)
            for j in range(NJ):
                if j >= BANKS:
                    pe.wait_ge(period_kept, j - BANKS + 1)
                nc.tensor.matmul(conv[:, j % BANKS, 0:C], select_t[:, j, :], taps_t,
                                 start=True, stop=True).then_inc(period_made, 1)
            pe.wait_ge(ones_set, 1)
            pe.wait_ge(pads_set, 4)

            def mean_sum(t):
                pe.wait_ge(stat_step, after(t, "sum_means"))
                nc.tensor.matmul(sum_mean_ps, ones[:, :], sum_means[:, :], start=True, stop=True)\
                    .then_inc(stat_sums, 1)

            def m2_sum(t):
                pe.wait_ge(stat_step, after(t, "sum_m2"))
                nc.tensor.matmul(sum_m2_ps, ones[:, :], sum_m2[:, :], start=True, stop=True)\
                    .then_inc(stat_sums, 1)

            def quads(g, last):
                for k in range(SLOTS):
                    t = g * SLOTS + k
                    pe.wait_ge(hi_made, t * QB + QB)
                    pe.wait_ge(lo_made, t * QB + QB)
                    for c in range(CG):
                        if k == 0:
                            pe.wait_ge(band_hi_made, g * CG + c + 1)
                            pe.wait_ge(band_lo_made, g * CG + c + 1)
                        pe.wait_ge(bank_free, t * CG + c + 1)
                        bank = conv[:, c % BANKS, :]
                        n = 0
                        for dx in range(DX):
                            for part, moving in ((0, hi), (0, lo), (1, hi)):
                                mm = nc.tensor.matmul(bank, bands[:, c, part, dx, 0:P],
                                                      moving[:, k % 2, :, c, dx:dx + W],
                                                      start=(n == 0), stop=(n == 3 * DX - 1))
                                n += 1
                        mm.then_inc(conv_made, 1)
                        if not (last and k == SLOTS - 1):
                            if c == 1:
                                mean_sum(t + 1)
                            if c == 2:
                                m2_sum(t + 1)

            mean_sum(0)
            m2_sum(0)
            with pe.Fori(0, G - 1) as g:
                quads(g, False)
            quads(G - 1, True)

        @block.scalar
        def _(act):
            def normalise(t, k):
                act.wait_ge(stat_step, after(t, "shift"))
                if not isinstance(t, int) or t >= 2:
                    act.wait_ge(conv_made, (t - 1) * CG)
                for b in range(QB):
                    v = t * QB + b
                    if not isinstance(v, int) or v >= 2:
                        act.wait_ge(lo_made, v - 1)
                    src = xt[:, k, b]
                    s, m = scale[:, k % 2, b:b + 1], shift[:, k % 2, b:b + 1]
                    nc.scalar.activation(xn[:, b % 2], src, ACT.Identity, scale=s, bias=m).then_inc(xn_made, 1)
                    nc.scalar.activation(hi[:, k % 2, b, :, 2:2 + W], src, ACT.Identity, scale=s, bias=m)\
                        .then_inc(hi_made, 1)

            def take_root(t):
                act.wait_ge(stat_step, after(t, "var"))
                nc.scalar.activation(root[:, :], var[:, :], ACT.Sqrt).then_inc(root_done, 1)

            def quads(g, last):
                for k in range(SLOTS):
                    if not (last and k == SLOTS - 1):
                        t = g * SLOTS + k + 1
                        take_root(t)
                        normalise(t, (k + 1) % SLOTS)

            take_root(0)
            normalise(0, 0)
            with act.Fori(0, G - 1) as g:
                quads(g, False)
            quads(G - 1, True)

        @block.gpsimd
        def _(pool):
            for buf in (hi, lo):
                v = buf[:, :, :, :, :].bitcast(F32).rearrange("p n b c w -> p (n b c) w")
                nc.gpsimd.memset(v[:, :, 0:2], 0.0).then_inc(pads_set, 1)
                nc.gpsimd.memset(v[:, :, 2 + W:WP], 0.0).then_inc(pads_set, 1)
            mask_v = mask[:, :].rearrange("p (a r) -> p a r", r=PERIOD).unsqueeze(1)\
                .broadcast_to([P, DX, BW // PERIOD, PERIOD])

            def band_lo(g, c):
                pool.wait_ge(period_split, g * 2 + 2)
                per = per_lo[:, c, :].bitcast(F32).rearrange("p (d r) -> p d r", r=PERIOD).unsqueeze(2)\
                    .broadcast_to([P, DX, BW // PERIOD, PERIOD])
                dst = bands[:, c, 1].rearrange("p d (a r) -> p d a r", r=PERIOD)
                nc.gpsimd.tensor_tensor(dst, mask_v, per, ALU.mult).then_inc(band_lo_made, 1)

            def rest(t, k):
                if not isinstance(t, int) or t >= 2:
                    pool.wait_ge(conv_made, (t - 1) * CG)
                for b in range(QB):
                    pool.wait_ge(xn_made, t * QB + b + 1)
                    pool.wait_ge(hi_made, t * QB + b + 1)
                    nc.gpsimd.tensor_tensor(lo[:, k % 2, b, :, 2:2 + W], xn[:, b % 2],
                                            hi[:, k % 2, b, :, 2:2 + W].bitcast(F32), ALU.subtract)\
                        .then_inc(lo_made, 1)

            def quads(g, last):
                for k in range(SLOTS):
                    t = g * SLOTS + k
                    if k == SLOTS - 1 and not last:
                        for c in range(CG // 2):
                            pool.wait_ge(conv_made, t * CG + c + 1)
                            band_lo(g + 1, c)
                    if not (last and k == SLOTS - 1):
                        rest(t + 1, (k + 1) % SLOTS)
                    if k == SLOTS - 1 and not last:
                        for c in range(CG // 2, CG):
                            pool.wait_ge(conv_made, t * CG + c + 1)
                            band_lo(g + 1, c)

            pool.wait_ge(consts_in, 48)
            for c in range(CG):
                band_lo(0, c)
            pool.wait_ge(pads_set, 4)
            rest(0, 0)
            with pool.Fori(0, G - 1) as g:
                quads(g, False)
            quads(G - 1, True)

        @block.vector
        def _(dve):
            nc.vector.memset(ones[:, :], 1.0).then_inc(ones_set, 1)
            mask_v = mask[:, :].rearrange("p (a r) -> p a r", r=PERIOD).unsqueeze(1)\
                .broadcast_to([P, DX, BW // PERIOD, PERIOD])
            periods_g = periods[:, :, :].rearrange("p (g c) j -> p g c j", c=CG)

            def bn_part(t, g, k, n):
                if n == 0:
                    dve.wait_ge(loaded[k], (g * 16 + 16) * QB)
                b, half = n // 2, n % 2
                src = xt[:, k, b, half * (CG // 2):(half + 1) * (CG // 2), :].rearrange("p c w -> p (c w)")
                nc.vector.bn_stats(bn[:, k % 2, b, half, :], src).then_inc(bn_done, 1)

            def bn_view(k, what):
                v = bn[:, k % 2].rearrange("p b f (e s) -> p b (f e) s", s=3)
                return v[:, :, :, what]

            def stat_a(t, k):
                dve.wait_ge(bn_done, t * 2 * QB + 2 * QB)
                nc.vector.tensor_reduce(sum_means[:, :], bn_view(k, 1), AX_X, ALU.add).then_inc(stat_step, 1)

            def stat_b(t, k):
                dve.wait_ge(stat_sums, t * 2 + 1)
                nc.vector.tensor_scalar(mean[:, :], sum_mean_ps, 1.0 / N_MEANS, None, ALU.mult)\
                    .then_inc(stat_step, 1)
                dve.wait_ge(stat_step, after(t, "mean"))
                nc.vector.tensor_tensor(diff[:, :, :], bn_view(k, 1),
                                        mean[:, :].unsqueeze(2).broadcast_to([P, QB, SUBS]),
                                        ALU.subtract).then_inc(stat_step, 1)
                dve.wait_ge(stat_step, after(t, "diff"))
                nc.vector.scalar_tensor_tensor(out=diff2[:, :, :], in0=diff[:, :, :], scalar=float(SUB_COUNT),
                                               in1=diff[:, :, :], op0=ALU.mult, op1=ALU.mult)\
                    .then_inc(stat_step, 1)
                dve.wait_ge(stat_step, after(t, "diff2"))
                nc.vector.tensor_tensor(m2[:, :, :], diff2[:, :, :], bn_view(k, 2), ALU.add)\
                    .then_inc(stat_step, 1)
                dve.wait_ge(stat_step, after(t, "m2"))
                nc.vector.tensor_reduce(sum_m2[:, :], m2[:, :, :], AX_X, ALU.add).then_inc(stat_step, 1)

            def stat_c(t):
                dve.wait_ge(stat_sums, t * 2 + 2)
                nc.vector.tensor_scalar(var[:, :], sum_m2_ps, 1.0 / N_ALL, EPS, ALU.mult, ALU.add)\
                    .then_inc(stat_step, 1)

            def stat_d(t, k):
                dve.wait_ge(root_done, t + 1)
                nc.vector.reciprocal(inv[:, :], root[:, :]).then_inc(stat_step, 1)
                dve.wait_ge(stat_step, after(t, "inv"))
                nc.vector.tensor_tensor(inv2[:, :], inv[:, :], inv[:, :], ALU.mult).then_inc(stat_step, 1)
                dve.wait_ge(stat_step, after(t, "inv2"))
                nc.vector.tensor_tensor(ratio[:, :], inv2[:, :], var[:, :], ALU.mult).then_inc(stat_step, 1)
                dve.wait_ge(stat_step, after(t, "ratio"))
                nc.vector.tensor_scalar(corr[:, :], ratio[:, :], -0.5, 1.5, ALU.mult, ALU.add)\
                    .then_inc(stat_step, 1)
                dve.wait_ge(stat_step, after(t, "corr"))
                nc.vector.tensor_tensor(scale[:, k % 2, :], inv[:, :], corr[:, :], ALU.mult)\
                    .then_inc(stat_step, 1)
                dve.wait_ge(stat_step, after(t, "scale"))
                nc.vector.scalar_tensor_tensor(out=shift[:, k % 2, :], in0=mean[:, :], scalar=-1.0,
                                               in1=scale[:, k % 2, :], op0=ALU.mult, op1=ALU.mult)\
                    .then_inc(stat_step, 1)

            def split_periods(g):
                if not isinstance(g, int) or g >= 1:
                    dve.wait_ge(band_lo_made, g * CG)
                nc.vector.tensor_copy(per_hi[:, :, :], periods_g[:, g]).then_inc(period_split, 1)
                dve.wait_ge(period_split, g * 2 + 1)
                nc.vector.tensor_tensor(per_lo[:, :, :], periods_g[:, g], per_hi[:, :, :].bitcast(F32),
                                        ALU.subtract).then_inc(period_split, 1)

            def band_hi(g, c):
                per = periods_g[:, g, c].rearrange("p (d r) -> p d r", r=PERIOD).unsqueeze(2)\
                    .broadcast_to([P, DX, BW // PERIOD, PERIOD])
                dst = bands[:, c, 0].rearrange("p d (a r) -> p d a r", r=PERIOD)
                nc.vector.tensor_tensor(dst, mask_v, per, ALU.mult).then_inc(band_hi_made, 1)

            def add_conv(t, k, c):
                dve.wait_ge(conv_made, t * CG + c + 1)
                dst = xt[:, k, :, c, :]
                nc.vector.tensor_tensor(dst, conv[:, c % BANKS, :].rearrange("p (b w) -> p b w", b=QB), dst,
                                        ALU.add).then_inc(bank_free, 1)

            def quads(g, last):
                for k in range(SLOTS):
                    t = g * SLOTS + k
                    ahead = not (last and k == SLOTS - 1)
                    k1, k2 = (k + 1) % SLOTS, (k + 2) % SLOTS
                    for c in range(CG):
                        if not last or k + 2 < SLOTS:
                            bn_part(t + 2, g + (k + 2) // SLOTS, k2, c)
                        add_conv(t, k, c)
                        if c == 0 and ahead:
                            stat_a(t + 1, k1)
                        if c == 1 and ahead:
                            stat_b(t + 1, k1)
                        if c == 2 and ahead:
                            stat_c(t + 1)
                            stat_d(t + 1, k1)
                        if k == SLOTS - 1 and not last:
                            band_hi(g + 1, c)
                    if k == SLOTS - 2 and not last:
                        split_periods(g + 1)

            dve.wait_ge(consts_in, 48)
            for j in range(NJ):
                dve.wait_ge(period_made, j + 1)
                nc.vector.tensor_copy(periods[:, :, j], conv[:, j % BANKS, 0:C]).then_inc(period_kept, 1)
            dve.wait_ge(period_kept, NJ)
            split_periods(0)
            for c in range(CG):
                band_hi(0, c)
            for n in range(2 * QB):
                bn_part(0, 0, 0, n)
            stat_a(0, 0)
            stat_b(0, 0)
            stat_c(0)
            stat_d(0, 0)
            for n in range(2 * QB):
                bn_part(1, 0, 1, n)
            dve.sem_inc(bank_free, BANKS)
            with dve.Fori(0, G - 1) as g:
                quads(g, False)
            quads(G - 1, True)


def tap_selection():
    s = np.zeros((TAPS, DX, PERIOD, P), np.float32)
    for dx in range(DX):
        for r in range(PERIOD):
            for k in range(P):
                dh = (k - r + 2) % PERIOD
                at = DX * dh + dx
                if at in POS:
                    s[POS.index(at), dx, r, k] = 1.0
                if at in NEG:
                    s[NEG.index(at), dx, r, k] = -1.0
    return s.reshape(TAPS, DX * PERIOD, P)


def band_positions():
    m = np.zeros((P, (P + PERIOD - 1) // PERIOD * PERIOD), np.float32)
    for k in range(P):
        m[k, max(0, k - 2):min(P, k + 3)] = 1.0
    return m


def kernel(x, L0_conv_weight):
    import numpy as _np
    import concourse.bacc as _bacc
    from concourse import mybir as _mybir
    from concourse.bass_utils import run_bass_kernel_spmd as _run

    nc = _bacc.Bacc("TRN2", target_bir_lowering=False, num_devices=1)
    arrays = {
        "x_dram": _np.ascontiguousarray(x),
        "taps_dram": _np.ascontiguousarray(_np.asarray(L0_conv_weight).reshape(-1, TAPS + 1)[:, 1:].T),
        "tap_select_dram": tap_selection(),
        "band_mask_dram": band_positions(),
    }
    args = [nc.dram_tensor(n, a.shape, _mybir.dt.from_np(a.dtype), kind="ExternalInput").ap()
            for n, a in arrays.items()]
    out = nc.dram_tensor("out_dram", arrays["x_dram"].shape, _mybir.dt.float32, kind="ExternalOutput").ap()
    preact_conv(nc, *args, out)
    r = _run(nc, [arrays], core_ids=[0])
    return r.results[0]["out_dram"]
```

```python
from contextlib import ExitStack

import numpy as np

import concourse.bass as bass
from concourse import mybir

F32 = mybir.dt.float32
F32R = mybir.dt.float32r
ALU = mybir.AluOpType
ACT = mybir.ActivationFunctionType

P = 128
BLK = 32
QR = P // BLK
HALO = 2
OUTW = BLK - 2 * HALO
TAPS = 8
PERIOD = 5
DH = 5
DIAGS = DH + QR - 1
CG = 8
QB = 4
SLOTS = 4
PAIRS = CG // 2
RING = 4
AHEAD = 2
BANKS = 2
EPS = 1e-5

POS = [0, 2, 4, 10, 14, 20, 22, 24]
NEG = [6, 7, 8, 11, 13, 16, 17, 18]

SCALE_STEPS = ["var", "inv", "inv2", "ratio", "corr", "scale"]


def after(t, step):
    return t * len(SCALE_STEPS) + (SCALE_STEPS.index(step) + 1)


def preact_conv(nc, x, taps, tap_select, band_mask, out):
    B, C, H, W = x.shape
    G = C // CG
    assert H == P and B // QB == SLOTS
    NBLK = -(-W // OUTW)
    WP = NBLK * OUTW
    GAP = WP - W
    ROWS = QB * NBLK
    IS = BLK + 2
    HALF = ROWS // 2 * BLK
    REPS = -(-OUTW // PERIOD)
    NJ = DH * PERIOD
    N_ALL = CG * H * W

    x_q = x.rearrange("(k b) (g c) (i q) w -> g k b q i c w", b=QB, c=CG, q=QR)
    out_q = out.rearrange("(k b) (g c) (i q) w -> g k b q i c w", b=QB, c=CG, q=QR)

    with ExitStack() as ctx:
        def sb(name, shape, dt=F32):
            return ctx.enter_context(nc.sbuf_tensor(name, shape, dt))

        def sem(name):
            return ctx.enter_context(nc.semaphore(name))

        SLOT = CG * QB * WP + 2 * HALO
        xt = sb("xt", [P, SLOTS, SLOT])
        patches = sb("patches", [P, 2, 2 * ROWS, IS])
        hi = sb("hi", [P, RING, 2 * ROWS, IS], F32R)
        lo = sb("lo", [P, RING, 2 * ROWS, IS], F32R)
        z = sb("z", [P, 2, QB, CG // 2 * NBLK, BLK])
        bands = sb("bands", [P, CG, 2, 3 * QR, BLK], F32R)
        periods = sb("periods", [P, C, NJ])
        per_hi = sb("per_hi", [P, CG, DIAGS * PERIOD], F32R)
        per_lo = sb("per_lo", [P, CG, DIAGS * PERIOD], F32R)
        mask = sb("mask", [P, REPS * PERIOD])
        ones = sb("ones", [P, P])
        sum_x = sb("sum_x", [P, 2, QB])
        sum_d2 = sb("sum_d2", [P, 2, QB])
        mean = sb("mean", [P, SLOTS, QB])
        neg_mean = sb("neg_mean", [P, SLOTS, QB])
        var = sb("var", [P, QB])
        root = sb("root", [P, QB])
        inv = sb("inv", [P, QB])
        inv2 = sb("inv2", [P, QB])
        ratio = sb("ratio", [P, QB])
        corr = sb("corr", [P, QB])
        spare = sb("spare", [P, 1])
        scale = sb("scale", [P, SLOTS, QB])
        scratch = xt[0:TAPS, SLOTS - 2:SLOTS].rearrange("p k n -> p (k n)")
        select_t = scratch[:, 0:NJ * P].rearrange("t (j k) -> t j k", j=NJ)
        taps_t = scratch[:, NJ * P:NJ * P + C]

        conv = ctx.enter_context(nc.psum_tensor("conv", [P, BANKS, 2, 512], F32))
        mean_ps = ctx.enter_context(nc.psum_tensor("mean_ps", [P, 512], F32))
        var_ps = ctx.enter_context(nc.psum_tensor("var_ps", [P, 512], F32))
        unused = ctx.enter_context(nc.psum_tensor("unused", [P, CG, W], F32))

        loaded = [sem(f"loaded{k}") for k in range(SLOTS)]
        stored = sem("stored")
        consts_in = sem("consts_in")
        ones_set = sem("ones_set")
        zeros_set = sem("zeros_set")
        period_made = sem("period_made")
        period_kept = sem("period_kept")
        per_hi_made = sem("per_hi_made")
        per_lo_made = sem("per_lo_made")
        band_hi_made = sem("band_hi_made")
        band_lo_made = sem("band_lo_made")
        sum_made = sem("sum_made")
        d2_made = sem("d2_made")
        mean_summed = sem("mean_summed")
        d2_summed = sem("d2_summed")
        mean_made = sem("mean_made")
        scale_step = sem("scale_step")
        root_done = sem("root_done")
        border_set = sem("border_set")
        patches_made = sem("patches_made")
        ends_set = sem("ends_set")
        hi_made = sem("hi_made")
        lo_made = sem("lo_made")
        conv_made = sem("conv_made")
        bank_free = sem("bank_free")
        added = sem("added")

        def x_cols(k, first, n):
            at = xt[:, k, HALO + first:HALO + first + 1]
            return bass.AP(tensor=at.tensor, offset=at.offset, ap=[at.ap[0], [CG * WP, QB], [WP, CG], [1, n]])

        def slot_image(k, b):
            return x_cols(k, 0, W)[:, b]

        def bands_of(c, part):
            return bands[:, c, part, 2:2 + DIAGS, 0:REPS * PERIOD].rearrange("p e (a r) -> p e a r", r=PERIOD)

        def repeated(v):
            return v.rearrange("p (e r) -> p e r", r=PERIOD).unsqueeze(2).broadcast_to([P, DIAGS, REPS, PERIOD])

        def mask_of():
            return mask[:, :].rearrange("p (a r) -> p a r", r=PERIOD).unsqueeze(1)\
                .broadcast_to([P, DIAGS, REPS, PERIOD])

        periods_g = periods[:, :, :].rearrange("p (g c) j -> p g c j", c=CG)

        block = ctx.enter_context(nc.Block())

        @block.sync
        def _(sp):
            def load(g, k):
                for b in range(QB):
                    for q in range(QR):
                        sp.dma_start(slot_image(k, b)[q * BLK:(q + 1) * BLK], x_q[g, k, b, q])\
                            .then_inc(loaded[k], 16)

            def store(g, k):
                t = g * SLOTS + k
                for b in range(QB):
                    sp.wait_ge(added, t * 2 * QB + QB + b + 1)
                    for q in range(QR):
                        sp.dma_start(out_q[g, k, b, q], slot_image(k, b)[q * BLK:(q + 1) * BLK])\
                            .then_inc(stored, 16)
                sp.wait_ge(stored, (t * 16 + 16) * QB * QR)

            sp.dma_start(select_t, tap_select).then_inc(consts_in, 16)
            sp.dma_start(taps_t, taps).then_inc(consts_in, 16)
            sp.dma_start(mask[:, :], band_mask).then_inc(consts_in, 16)
            for k in range(SLOTS):
                if k == SLOTS - 2:
                    sp.wait_ge(period_made, NJ)
                load(0, k)
            with sp.Fori(0, G - 1) as g:
                for k in range(SLOTS):
                    store(g, k)
                    load(g + 1, k)
            for k in range(SLOTS):
                store(G - 1, k)

        @block.tensor
        def _(pe):
            pe.wait_ge(consts_in, 48)
            for j in range(NJ):
                if j >= 2 * BANKS:
                    pe.wait_ge(period_kept, j - 2 * BANKS + 1)
                nc.tensor.matmul(conv[:, j // 2 % BANKS, j % 2, 0:C], select_t[:, j, :], taps_t,
                                 start=True, stop=True).then_inc(period_made, 1)
            pe.wait_ge(ones_set, 1)

            def mean_sum(t, k):
                pe.wait_ge(sum_made, t * QB + QB)
                nc.tensor.matmul(mean_ps[:, 0:QB], ones[:, :], sum_x[:, k % 2, :], start=True, stop=True)\
                    .then_inc(mean_summed, 1)

            def d2_sum(t, k):
                pe.wait_ge(d2_made, t * QB + QB)
                nc.tensor.matmul(var_ps[:, 0:QB], ones[:, :], sum_d2[:, k % 2, :], start=True, stop=True)\
                    .then_inc(d2_summed, 1)

            def quads(g, first, last):
                for k in range(SLOTS):
                    t = g * SLOTS + k
                    for c in range(CG):
                        if k == 0:
                            pe.wait_ge(band_hi_made, g * CG + c + 1)
                            pe.wait_ge(band_lo_made, g * CG + c + 1)
                        if c % 2 == 0:
                            pe.wait_ge(lo_made, t * PAIRS + c // 2 + 1)
                        pe.wait_ge(bank_free, t * CG + c + 1)
                        n = 0
                        for shift in (1, 0, -1):
                            e = QR * (1 - shift)
                            for part, moving in ((0, hi), (0, lo), (1, hi)):
                                pair = moving[:, (k * PAIRS + c // 2) % RING].rearrange(
                                    "p (b n) i -> p b n i", b=QB)
                                for half in range(2):
                                    mm = nc.tensor.matmul(
                                        conv[:, c % BANKS, half, 0:HALF],
                                        bands[:, c, part, e:e + QR, :],
                                        pair[:, half * (QB // 2):(half + 1) * (QB // 2),
                                             c % 2 * NBLK:(c % 2 + 1) * NBLK, 1 + shift:1 + shift + BLK],
                                        start=(n == 0), stop=(n == 8))
                                n += 1
                        mm.then_inc(conv_made, 1)
                        if c == 0:
                            d2_sum(t, k)
                        if c == 1 and not (last and k + 1 >= SLOTS):
                            mean_sum(t + 1, k + 1)

            mean_sum(0, 0)
            quads(0, True, False)
            with pe.Fori(1, G - 1) as g:
                quads(g, False, False)
            quads(G - 1, False, True)

        @block.scalar
        def _(act):
            def sums(t, g, k, images):
                act.wait_ge(loaded[k % SLOTS], (g * 16 + 16) * QB * QR)
                for b in images:
                    if b > 0:
                        act.wait_ge(sum_made, t * QB + b)
                    elif not isinstance(t, int) or t > 0:
                        act.wait_ge(d2_made, t * QB)
                    nc.scalar.activation(unused[:, :, :], slot_image(k % SLOTS, b), ACT.Identity,
                                         accum_out=sum_x[:, k % 2, b:b + 1]).then_inc(sum_made, 1)

            def squares(t, k, images):
                act.wait_ge(mean_made, t * 2 + 2)
                for b in images:
                    if b > 0:
                        act.wait_ge(d2_made, t * QB + b)
                    nc.scalar.activation(unused[:, :, :], slot_image(k % SLOTS, b), ACT.Square,
                                         bias=neg_mean[:, k % SLOTS, b:b + 1],
                                         accum_out=sum_d2[:, k % 2, b:b + 1]).then_inc(d2_made, 1)

            def take_root(t):
                act.wait_ge(scale_step, after(t, "var"))
                nc.scalar.activation(root[:, :], var[:, :], ACT.Sqrt).then_inc(root_done, 1)

            def ends(n, buffer, k, quad):
                if not isinstance(n, int) or n >= 2:
                    act.wait_ge(lo_made, n - 1)
                act.wait_ge(mean_made, quad * 2 + 1)
                m = mean[:, k % SLOTS, :].unsqueeze(2).unsqueeze(3).broadcast_to([P, QB, 2 * NBLK, 2])
                v = patches[:, buffer].rearrange("p (b n) i -> p b n i", b=QB)
                nc.scalar.activation(v[:, :, :, 0:IS:IS - 1], m, ACT.Identity).then_inc(ends_set, 1)

            def split_hi(n, slot, quad):
                if slot % PAIRS < 2:
                    ends(n, slot % PAIRS, slot // PAIRS, quad)
                    act.wait_ge(ends_set, quad * 2 + slot % PAIRS + 1)
                act.wait_ge(patches_made, n + 1)
                if not isinstance(n, int) or n >= RING:
                    act.wait_ge(bank_free, (n - RING) * 2 + 2 + BANKS)
                nc.scalar.activation(hi[:, slot % RING], patches[:, slot % 2], ACT.Identity).then_inc(hi_made, 1)

            def round_periods(g):
                if not isinstance(g, int) or g >= 1:
                    act.wait_ge(band_hi_made, g * CG)
                    act.wait_ge(per_lo_made, g * QR)
                for q in range(QR):
                    part = slice(q * BLK, (q + 1) * BLK)
                    nc.scalar.activation(per_hi[part, :, q * PERIOD:q * PERIOD + NJ], periods_g[part, g],
                                         ACT.Identity).then_inc(per_hi_made, 1)

            def quads(g, first, last):
                nc.scalar.activation(spare[:, :], ones[:, 0:1], ACT.Sqrt)
                for k in range(SLOTS):
                    t = g * SLOTS + k
                    ahead = not (last and k + 1 >= SLOTS)
                    for p in range(PAIRS):
                        if not (last and k * PAIRS + p + AHEAD >= SLOTS * PAIRS):
                            split_hi(t * PAIRS + p + AHEAD, k * PAIRS + p + AHEAD, t + (p + AHEAD) // PAIRS)
                        if p == 0 and ahead:
                            sums(t + 1, g + (k + 1) // SLOTS, k + 1, range(QB - 1, QB))
                        if p == 1:
                            take_root(t)
                        if p in (1, 2) and ahead:
                            squares(t + 1, k + 1, range((p - 1) * (QB // 2), p * (QB // 2)))
                        if p == 3 and not (last and k + 2 >= SLOTS):
                            sums(t + 2, g + (k + 2) // SLOTS, k + 2, range(QB - 1))
                    if k == SLOTS - 2 and not last:
                        round_periods(g + 1)

            act.wait_ge(zeros_set, SLOTS + 3)
            act.wait_ge(period_kept, NJ)
            round_periods(0)
            sums(0, 0, 0, range(QB))
            squares(0, 0, range(QB))
            for n in range(AHEAD):
                split_hi(n, n, 0)
            sums(1, 0, 1, range(QB - 1))
            quads(0, True, False)
            with act.Fori(1, G - 1) as g:
                quads(g, False, False)
            quads(G - 1, False, True)

        @block.gpsimd
        def _(pool):
            for k in range(SLOTS - 2):
                nc.gpsimd.memset(xt[:, k, CG * QB * WP:], 0.0).then_inc(zeros_set, 1)
            nc.gpsimd.memset(per_hi[:, :, :].bitcast(F32), 0.0).then_inc(zeros_set, 1)
            nc.gpsimd.memset(per_lo[:, :, :].bitcast(F32), 0.0).then_inc(zeros_set, 1)

            def rest_of_periods(g):
                if not isinstance(g, int) or g >= 1:
                    pool.wait_ge(band_lo_made, g * CG)
                    pool.wait_ge(lo_made, (g * SLOTS - 1) * PAIRS + AHEAD)
                for q in range(QR):
                    if q > 0:
                        pool.wait_ge(per_lo_made, g * QR + q)
                    pool.wait_ge(per_hi_made, g * QR + q + 1)
                    part, at = slice(q * BLK, (q + 1) * BLK), slice(q * PERIOD, q * PERIOD + NJ)
                    nc.gpsimd.tensor_tensor(per_lo[part, :, at], periods_g[part, g],
                                            per_hi[part, :, at].bitcast(F32), ALU.subtract)\
                        .then_inc(per_lo_made, 1)

            def band_lo(g, c):
                pool.wait_ge(per_lo_made, g * QR + QR)
                nc.gpsimd.tensor_tensor(bands_of(c, 1), mask_of(), repeated(per_lo[:, c, :].bitcast(F32)),
                                        ALU.mult).then_inc(band_lo_made, 1)

            def rest(n, slot):
                pool.wait_ge(hi_made, n + 1)
                nc.gpsimd.tensor_tensor(lo[:, slot % RING], patches[:, slot % 2],
                                        hi[:, slot % RING].bitcast(F32), ALU.subtract).then_inc(lo_made, 1)

            def quads(g, first, last):
                for k in range(SLOTS):
                    t = g * SLOTS + k
                    if k == SLOTS - 1 and not last:
                        rest_of_periods(g + 1)
                        pool.wait_ge(per_lo_made, (g + 2) * QR)
                    for p in range(PAIRS):
                        n, slot = t * PAIRS + p + AHEAD, k * PAIRS + p + AHEAD
                        if not (last and slot >= SLOTS * PAIRS):
                            rest(n, slot)
                        if k == SLOTS - 1 and not last and p > 0:
                            pool.wait_ge(conv_made, t * CG + 2 * p)
                            band_lo(g + 1, 2 * p - 2)
                            band_lo(g + 1, 2 * p - 1)
                        if k == 0 and p == 0 and not first:
                            pool.wait_ge(conv_made, t * CG)
                            band_lo(g, CG - 2)
                            band_lo(g, CG - 1)

            pool.wait_ge(consts_in, 48)
            pool.wait_ge(period_made, NJ)
            for k in range(SLOTS - 2, SLOTS):
                nc.gpsimd.memset(xt[:, k, CG * QB * WP:], 0.0).then_inc(zeros_set, 1)
            pool.wait_ge(zeros_set, SLOTS + 3)
            rest_of_periods(0)
            for c in range(CG):
                band_lo(0, c)
            for n in range(AHEAD):
                rest(n, n)
            quads(0, True, False)
            with pool.Fori(1, G - 1) as g:
                quads(g, False, False)
            quads(G - 1, False, True)

        @block.vector
        def _(dve):
            def make_mean(t, k):
                dve.wait_ge(mean_summed, t + 1)
                nc.vector.tensor_scalar(mean[:, k % SLOTS, :], mean_ps[:, 0:QB], 1.0 / N_ALL, None, ALU.mult)\
                    .then_inc(mean_made, 1)
                nc.vector.tensor_scalar(neg_mean[:, k % SLOTS, :], mean_ps[:, 0:QB], -1.0 / N_ALL, None, ALU.mult)\
                    .then_inc(mean_made, 1)

            def make_var(t):
                dve.wait_ge(d2_summed, t + 1)
                nc.vector.tensor_scalar(var[:, :], var_ps[:, 0:QB], 1.0 / N_ALL, EPS, ALU.mult, ALU.add)\
                    .then_inc(scale_step, 1)

            def make_scale(t, k):
                dve.wait_ge(root_done, t + 1)
                nc.vector.reciprocal(inv[:, :], root[:, :]).then_inc(scale_step, 1)
                dve.wait_ge(scale_step, after(t, "inv"))
                nc.vector.tensor_tensor(inv2[:, :], inv[:, :], inv[:, :], ALU.mult).then_inc(scale_step, 1)
                dve.wait_ge(scale_step, after(t, "inv2"))
                nc.vector.tensor_tensor(ratio[:, :], inv2[:, :], var[:, :], ALU.mult).then_inc(scale_step, 1)
                dve.wait_ge(scale_step, after(t, "ratio"))
                nc.vector.tensor_scalar(corr[:, :], ratio[:, :], -0.5, 1.5, ALU.mult, ALU.add)\
                    .then_inc(scale_step, 1)
                dve.wait_ge(scale_step, after(t, "corr"))
                nc.vector.tensor_tensor(scale[:, k % SLOTS, :], inv[:, :], corr[:, :], ALU.mult)\
                    .then_inc(scale_step, 1)

            def set_border(t, k):
                dve.wait_ge(mean_made, t * 2 + 2)
                m = mean[:, k % SLOTS, :].unsqueeze(2).unsqueeze(3)
                nc.vector.tensor_copy(x_cols(k % SLOTS, W, GAP), m.broadcast_to([P, QB, CG, GAP]))\
                    .then_inc(border_set, 1)
                dve.wait_ge(border_set, t * 2 + 1)
                nc.vector.tensor_copy(x_cols(k % SLOTS, -HALO, HALO)[:, :, 0:1], m.broadcast_to([P, QB, 1, HALO]))\
                    .then_inc(border_set, 1)

            def to_patches(n, slot, quad):
                k, c = slot // PAIRS % SLOTS, slot % PAIRS * 2
                if not isinstance(n, int) or n >= 2:
                    dve.wait_ge(lo_made, n - 1)
                dve.wait_ge(border_set, quad * 2 + 2)
                first = xt[:, k, c * WP:c * WP + 1]
                src = bass.AP(tensor=first.tensor, offset=first.offset,
                              ap=[first.ap[0], [CG * WP, QB], [OUTW, 2 * NBLK], [1, BLK]])
                nc.vector.transpose(patches[:, slot % 2, :, 1:1 + BLK], src).then_inc(patches_made, 1)

            def from_patches(t, k, c, first):
                dve.wait_ge(conv_made, t * CG + c + 1)
                if c == 0:
                    if not (first and k == 0):
                        dve.wait_ge(added, t * 2 * QB - QB)
                if c == CG // 2:
                    dve.wait_ge(added, t * 2 * QB)
                at = c % (CG // 2) * NBLK
                dst = z[:, c // (CG // 2), :, at:at + NBLK, :]
                nc.vector.transpose(dst, conv[:, c % BANKS, :, 0:HALF]).then_inc(bank_free, 1)

            def add(t, k, half, b):
                if half == 0 and b == 0:
                    dve.wait_ge(scale_step, after(t, "scale"))
                dve.wait_ge(bank_free, t * CG + (half + 1) * (CG // 2) + BANKS)
                at = (b * CG + half * (CG // 2)) * WP + HALO
                dst = xt[:, k, at:at + CG // 2 * WP].rearrange("p (n w) -> p n w", w=OUTW)
                nc.vector.scalar_tensor_tensor(out=dst, in0=z[:, half, b, :, 0:OUTW], scalar=scale[:, k, b:b + 1],
                                               in1=dst, op0=ALU.mult, op1=ALU.add).then_inc(added, 1)

            def band_hi(g, c):
                dve.wait_ge(per_hi_made, g * QR + QR)
                nc.vector.tensor_tensor(bands_of(c, 0), mask_of(), repeated(per_hi[:, c, :].bitcast(F32)), ALU.mult)\
                    .then_inc(band_hi_made, 1)

            def quads(g, first, last):
                for k in range(SLOTS):
                    t = g * SLOTS + k
                    for c in range(CG):
                        if c == 3 and not (last and k + 1 >= SLOTS):
                            set_border(t + 1, k + 1)
                        if c % 2 == 0 and not (last and k * PAIRS + c // 2 + AHEAD >= SLOTS * PAIRS):
                            to_patches(t * PAIRS + c // 2 + AHEAD, k * PAIRS + c // 2 + AHEAD,
                                       t + (c // 2 + AHEAD) // PAIRS)
                        from_patches(t, k, c, first)
                        if k == SLOTS - 1 and not last:
                            band_hi(g + 1, c)
                        if c < CG // 2 and not (first and k == 0):
                            add(t - 1, (k - 1) % SLOTS, 1, c)
                        if c >= CG // 2:
                            add(t, k, 0, c - CG // 2)
                        if c == 0:
                            make_var(t)
                        if c == 1 and not (last and k + 1 >= SLOTS):
                            make_mean(t + 1, k + 1)
                        if c == 3:
                            make_scale(t, k)
                if last:
                    for b in range(QB):
                        add(t, k, 1, b)

            nc.vector.memset(bands[:, :, :, :, :].bitcast(F32), 0.0).then_inc(zeros_set, 1)
            nc.vector.memset(ones[:, :], 1.0).then_inc(ones_set, 1)
            dve.wait_ge(consts_in, 48)
            for j in range(NJ):
                dve.wait_ge(period_made, j + 1)
                nc.vector.tensor_copy(periods[:, :, j], conv[:, j // 2 % BANKS, j % 2, 0:C]).then_inc(period_kept, 1)
            dve.wait_ge(zeros_set, SLOTS + 3)
            for c in range(CG):
                band_hi(0, c)
            make_mean(0, 0)
            set_border(0, 0)
            for n in range(AHEAD):
                to_patches(n, n, 0)
            dve.sem_inc(bank_free, BANKS)
            quads(0, True, False)
            with dve.Fori(1, G - 1) as g:
                quads(g, False, False)
            quads(G - 1, False, True)


def tap_selection():
    s = np.zeros((TAPS, DH, PERIOD, QR, BLK), np.float32)
    for d in range(DH):
        for r in range(PERIOD):
            for wi in range(BLK):
                at = 5 * (DH - 1 - d) + (wi - r) % PERIOD
                if at in POS:
                    s[POS.index(at), d, r, :, wi] = 1.0
                if at in NEG:
                    s[NEG.index(at), d, r, :, wi] = -1.0
    return s.reshape(TAPS, DH * PERIOD, P)


def band_positions():
    m = np.zeros((QR, BLK, -(-OUTW // PERIOD) * PERIOD), np.float32)
    for wi in range(BLK):
        m[:, wi, max(0, wi - 2 * HALO):min(OUTW, wi + 1)] = 1.0
    return m.reshape(P, -1)


def kernel(x, L0_conv_weight):
    import numpy as _np
    import concourse.bacc as _bacc
    from concourse import mybir as _mybir
    from concourse.bass_utils import run_bass_kernel_spmd as _run

    nc = _bacc.Bacc("TRN2", target_bir_lowering=False, num_devices=1)
    arrays = {
        "x_dram": _np.ascontiguousarray(x),
        "taps_dram": _np.ascontiguousarray(_np.asarray(L0_conv_weight).reshape(-1, TAPS + 1)[:, 1:].T),
        "tap_select_dram": tap_selection(),
        "band_mask_dram": band_positions(),
    }
    args = [nc.dram_tensor(n, a.shape, _mybir.dt.from_np(a.dtype), kind="ExternalInput").ap()
            for n, a in arrays.items()]
    out = nc.dram_tensor("out_dram", arrays["x_dram"].shape, _mybir.dt.float32, kind="ExternalOutput").ap()
    preact_conv(nc, *args, out)
    r = _run(nc, [arrays], core_ids=[0])
    return r.results[0]["out_dram"]
```

```python
from contextlib import ExitStack

import numpy as np

import concourse.bass as bass
from concourse import mybir

F32 = mybir.dt.float32
F32R = mybir.dt.float32r
ALU = mybir.AluOpType
ACT = mybir.ActivationFunctionType

P = 128
BLK = 32
QR = P // BLK
HALO = 2
OUTW = BLK - 2 * HALO
TAPS = 8
PERIOD = 5
DH = 5
DIAGS = DH + QR - 1
CG = 8
QB = 4
SLOTS = 4
PAIRS = CG // 2
RING = 4
AHEAD = 3
BANKS = 2
EPS = 1e-5

POS = [0, 2, 4, 10, 14, 20, 22, 24]
NEG = [6, 7, 8, 11, 13, 16, 17, 18]

SCALE_STEPS = ["inverse", "square", "ratio", "scale"]


def after(t, step):
    return t * len(SCALE_STEPS) + (SCALE_STEPS.index(step) + 1)


def preact_conv(nc, x, taps, tap_select, band_mask, out):
    B, C, H, W = x.shape
    G = C // CG
    assert H == P and B // QB == SLOTS
    NBLK = -(-W // OUTW)
    WP = NBLK * OUTW
    GAP = WP - W
    ROWS = QB * NBLK
    IS = BLK + 2
    HALF = ROWS // 2 * BLK
    REPS = -(-OUTW // PERIOD)
    NJ = DH * PERIOD
    N_ALL = CG * H * W

    x_q = x.rearrange("(k b) (g c) (i q) w -> g k b q i c w", b=QB, c=CG, q=QR)
    out_q = out.rearrange("(k b) (g c) (i q) w -> g k b q i c w", b=QB, c=CG, q=QR)

    with ExitStack() as ctx:
        def sb(name, shape, dt=F32):
            return ctx.enter_context(nc.sbuf_tensor(name, shape, dt))

        def sem(name):
            return ctx.enter_context(nc.semaphore(name))

        SLOT = CG * QB * WP + 2 * HALO
        xt = sb("xt", [P, SLOTS, SLOT])
        patches = sb("patches", [P, 2, 2 * ROWS, IS])
        hi = sb("hi", [P, RING, 2 * ROWS, IS], F32R)
        lo = sb("lo", [P, RING, 2 * ROWS, IS], F32R)
        z = sb("z", [P, 2, QB, CG // 2 * NBLK, BLK])
        bands = sb("bands", [P, CG, 2, 3 * QR, BLK], F32R)
        periods = sb("periods", [P, C, NJ])
        per_hi = sb("per_hi", [P, CG, DIAGS * PERIOD], F32R)
        per_lo = sb("per_lo", [P, CG, DIAGS * PERIOD], F32R)
        mask = sb("mask", [P, REPS * PERIOD])
        ones = sb("ones", [P, P])
        eps = sb("eps", [P, 1])
        sums = sb("sums", [P, 2, 2, QB])
        mean = sb("mean", [P, SLOTS, QB])
        var = sb("var", [P, QB])
        root = sb("root", [P, QB])
        inverse = sb("inverse", [P, QB])
        square = sb("square", [P, QB])
        ratio = sb("ratio", [P, QB])
        spare = sb("spare", [P, 1])
        scale = sb("scale", [P, SLOTS, QB])
        scratch = xt[0:TAPS, SLOTS - 2:SLOTS].rearrange("p k n -> p (k n)")
        select_t = scratch[:, 0:NJ * P].rearrange("t (j k) -> t j k", j=NJ)
        taps_t = scratch[:, NJ * P:NJ * P + C]

        conv = ctx.enter_context(nc.psum_tensor("conv", [P, BANKS, 2, 512], F32))
        totals = ctx.enter_context(nc.psum_tensor("totals", [P, 512 // QB, QB], F32))
        unused = ctx.enter_context(nc.psum_tensor("unused", [P, CG, W], F32))

        loaded = [sem(f"loaded{k}") for k in range(SLOTS)]
        stored = sem("stored")
        consts_in = sem("consts_in")
        ones_set = sem("ones_set")
        zeros_set = sem("zeros_set")
        period_made = sem("period_made")
        period_kept = sem("period_kept")
        per_hi_made = sem("per_hi_made")
        per_lo_made = sem("per_lo_made")
        band_hi_made = sem("band_hi_made")
        band_lo_made = sem("band_lo_made")
        sum_made = sem("sum_made")
        d2_made = sem("d2_made")
        totals_made = sem("totals_made")
        mean_made = sem("mean_made")
        root_made = sem("root_made")
        scale_step = sem("scale_step")
        border_set = sem("border_set")
        patches_made = sem("patches_made")
        ends_set = sem("ends_set")
        hi_made = sem("hi_made")
        lo_made = sem("lo_made")
        conv_made = sem("conv_made")
        bank_free = sem("bank_free")
        added = sem("added")

        def x_cols(k, first, n):
            at = xt[:, k, HALO + first:HALO + first + 1]
            return bass.AP(tensor=at.tensor, offset=at.offset, ap=[at.ap[0], [CG * WP, QB], [WP, CG], [1, n]])

        def slot_image(k, b):
            return x_cols(k, 0, W)[:, b]

        def bands_of(c, part):
            return bands[:, c, part, QR - HALO:QR - HALO + DIAGS, 0:REPS * PERIOD].rearrange("p e (a r) -> p e a r", r=PERIOD)

        def repeated(v):
            return v.rearrange("p (e r) -> p e r", r=PERIOD).unsqueeze(2).broadcast_to([P, DIAGS, REPS, PERIOD])

        def mask_of():
            return mask[:, :].rearrange("p (a r) -> p a r", r=PERIOD).unsqueeze(1)\
                .broadcast_to([P, DIAGS, REPS, PERIOD])

        periods_g = periods[:, :, :].rearrange("p (g c) j -> p g c j", c=CG)

        block = ctx.enter_context(nc.Block())

        @block.sync
        def _(sp):
            def load(g, k):
                for b in range(QB):
                    for q in range(QR):
                        sp.dma_start(slot_image(k, b)[q * BLK:(q + 1) * BLK], x_q[g, k, b, q])\
                            .then_inc(loaded[k], 16)

            def store(g, k):
                t = g * SLOTS + k
                for b in range(QB):
                    sp.wait_ge(added, (t * 2 + 1) * QB + b + 1)
                    for q in range(QR):
                        sp.dma_start(out_q[g, k, b, q], slot_image(k, b)[q * BLK:(q + 1) * BLK])\
                            .then_inc(stored, 16)
                sp.wait_ge(stored, (t * 16 + 16) * QB * QR)

            sp.dma_start(select_t, tap_select).then_inc(consts_in, 16)
            sp.dma_start(taps_t, taps).then_inc(consts_in, 16)
            sp.dma_start(mask[:, :], band_mask).then_inc(consts_in, 16)
            for k in range(SLOTS):
                if k == SLOTS - 2:
                    sp.wait_ge(period_made, NJ)
                load(0, k)
            with sp.Fori(0, G - 1) as g:
                for k in range(SLOTS):
                    store(g, k)
                    load(g + 1, k)
            for k in range(SLOTS):
                store(G - 1, k)

        @block.tensor
        def _(pe):
            pe.wait_ge(consts_in, 48)
            for j in range(NJ):
                if j >= 2 * BANKS:
                    pe.wait_ge(period_kept, j - 2 * BANKS + 1)
                nc.tensor.matmul(conv[:, j // 2 % BANKS, j % 2, 0:C], select_t[:, j, :], taps_t,
                                 start=True, stop=True).then_inc(period_made, 1)
            pe.wait_ge(ones_set, 2)

            def total(k, what):
                nc.tensor.matmul(totals[:, what, :], ones[:, :], sums[:, k % 2, what, :], start=True, stop=True)\
                    .then_inc(totals_made, 1)

            def quads(g, first, last):
                for k in range(SLOTS):
                    t = g * SLOTS + k
                    for c in range(CG):
                        if k == 0:
                            pe.wait_ge(band_hi_made, g * CG + c + 1)
                            pe.wait_ge(band_lo_made, g * CG + c + 1)
                        if c % 2 == 0:
                            pe.wait_ge(lo_made, t * PAIRS + c // 2 + 1)
                        pe.wait_ge(bank_free, t * CG + c + 1)
                        n = 0
                        for shift in (1, 0, -1):
                            e = QR * (1 - shift)
                            for part, moving in ((0, hi), (0, lo), (1, hi)):
                                pair = moving[:, (k * PAIRS + c // 2) % RING].rearrange(
                                    "p (b n) i -> p b n i", b=QB)
                                for half in range(2):
                                    mm = nc.tensor.matmul(
                                        conv[:, c % BANKS, half, 0:HALF],
                                        bands[:, c, part, e:e + QR, :],
                                        pair[:, half * (QB // 2):(half + 1) * (QB // 2),
                                             c % 2 * NBLK:(c % 2 + 1) * NBLK, 1 + shift:1 + shift + BLK],
                                        start=(n == 0), stop=(n == 8))
                                n += 1
                        mm.then_inc(conv_made, 1)
                        if c == 0:
                            pe.wait_ge(d2_made, t * QB + QB)
                            if last and k + 1 >= SLOTS:
                                total(k, slice(0, 1))
                            else:
                                pe.wait_ge(sum_made, (t + 1) * QB + QB)
                                total(k, slice(0, 2))

            pe.wait_ge(sum_made, QB)
            total(-1, slice(1, 2))
            quads(0, True, False)
            with pe.Fori(1, G - 1) as g:
                quads(g, False, False)
            quads(G - 1, False, True)

        @block.scalar
        def _(act):
            def sum_x(t, g, k, images):
                act.wait_ge(loaded[k % SLOTS], (g * 16 + 16) * QB * QR)
                for b in images:
                    if b > 0:
                        act.wait_ge(sum_made, t * QB + b)
                    elif not isinstance(t, int) or t > 0:
                        act.wait_ge(d2_made, t * QB)
                    nc.scalar.activation(unused[:, :, :], slot_image(k % SLOTS, b), ACT.Identity,
                                         accum_out=sums[:, (k - 1) % 2, 1, b:b + 1]).then_inc(sum_made, 1)

            def make_mean(t, k):
                act.wait_ge(totals_made, t + 1)
                nc.scalar.activation(mean[:, k % SLOTS, :], totals[:, 1, :], ACT.Identity, scale=1.0 / N_ALL)\
                    .then_inc(mean_made, 1)

            def set_border(t, k):
                act.wait_ge(mean_made, t + 1)
                m = mean[:, k % SLOTS, :].unsqueeze(2).unsqueeze(3)
                nc.scalar.activation(x_cols(k % SLOTS, W, GAP), m.broadcast_to([P, QB, CG, GAP]), ACT.Identity)\
                    .then_inc(border_set, 1)
                act.wait_ge(border_set, t * 2 + 1)
                nc.scalar.activation(x_cols(k % SLOTS, -HALO, HALO)[:, :, 0:1], m.broadcast_to([P, QB, 1, HALO]),
                                     ACT.Identity).then_inc(border_set, 1)

            def squares(t, k, images):
                act.wait_ge(mean_made, t + 1)
                for b in images:
                    if b > 0:
                        act.wait_ge(d2_made, t * QB + b)
                    nc.scalar.activation(unused[:, :, :], slot_image(k % SLOTS, b), ACT.Square,
                                         bias=mean[:, k % SLOTS, b:b + 1], scale=-1.0,
                                         accum_out=sums[:, k % 2, 0, b:b + 1]).then_inc(d2_made, 1)

            def take_root(t, first):
                act.wait_ge(totals_made, t + 2)
                if not first:
                    act.wait_ge(scale_step, after(t - 1, "scale"))
                nc.scalar.activation(var[:, :], totals[:, 0, :], ACT.Identity, bias=eps[:, :], scale=1.0 / N_ALL)\
                    .then_inc(root_made, 1)
                nc.scalar.activation(root[:, :], totals[:, 0, :], ACT.Sqrt, bias=eps[:, :], scale=1.0 / N_ALL)\
                    .then_inc(root_made, 1)

            def ends(n, buffer, k, quad):
                if not isinstance(n, int) or n >= 2:
                    act.wait_ge(lo_made, n - 1)
                act.wait_ge(mean_made, quad + 1)
                m = mean[:, k % SLOTS, :].unsqueeze(2).unsqueeze(3).broadcast_to([P, QB, 2 * NBLK, 2])
                v = patches[:, buffer].rearrange("p (b n) i -> p b n i", b=QB)
                nc.scalar.activation(v[:, :, :, 0:IS:IS - 1], m, ACT.Identity).then_inc(ends_set, 1)

            def split_hi(n, slot, quad):
                if slot % PAIRS < 2:
                    ends(n, slot % PAIRS, slot // PAIRS, quad)
                    act.wait_ge(ends_set, quad * 2 + slot % PAIRS + 1)
                act.wait_ge(patches_made, n + 1)
                if not isinstance(n, int) or n >= RING:
                    act.wait_ge(bank_free, (n - RING) * 2 + 2 + BANKS)
                nc.scalar.activation(hi[:, slot % RING], patches[:, slot % 2], ACT.Identity).then_inc(hi_made, 1)

            def round_periods(g):
                if not isinstance(g, int) or g >= 1:
                    act.wait_ge(band_hi_made, g * CG)
                    act.wait_ge(per_lo_made, g * QR)
                for q in range(QR):
                    part = slice(q * BLK, (q + 1) * BLK)
                    nc.scalar.activation(per_hi[part, :, q * PERIOD:q * PERIOD + NJ], periods_g[part, g],
                                         ACT.Identity).then_inc(per_hi_made, 1)

            def quads(g, first, last):
                nc.scalar.activation(spare[:, :], ones[:, 0:1], ACT.Sqrt)
                for k in range(SLOTS):
                    t = g * SLOTS + k
                    ahead = not (last and k + 1 >= SLOTS)
                    for p in range(PAIRS):
                        if not (last and k * PAIRS + p + AHEAD >= SLOTS * PAIRS):
                            split_hi(t * PAIRS + p + AHEAD, k * PAIRS + p + AHEAD, t + (p + AHEAD) // PAIRS)
                        half = range(p % 2 * (QB // 2), (p % 2 + 1) * (QB // 2))
                        if p == 0:
                            take_root(t, first and k == 0)
                        if p == 0 and ahead:
                            make_mean(t + 1, k + 1)
                            set_border(t + 1, k + 1)
                        if p < 2 and ahead:
                            squares(t + 1, k + 1, half)
                        if p >= 2 and not (last and k + 2 >= SLOTS):
                            sum_x(t + 2, g + (k + 2) // SLOTS, k + 2, half)
                    if k == SLOTS - 2 and not last:
                        round_periods(g + 1)

            sum_x(0, 0, 0, range(QB))
            act.wait_ge(zeros_set, SLOTS + 3)
            act.wait_ge(period_kept, NJ)
            round_periods(0)
            act.wait_ge(ones_set, 2)
            make_mean(0, 0)
            set_border(0, 0)
            split_hi(0, 0, 0)
            squares(0, 0, range(QB))
            for n in range(1, AHEAD):
                split_hi(n, n, 0)
            sum_x(1, 0, 1, range(QB))
            quads(0, True, False)
            with act.Fori(1, G - 1) as g:
                quads(g, False, False)
            quads(G - 1, False, True)

        @block.gpsimd
        def _(pool):
            nc.gpsimd.memset(bands[:, :, :, :, :].bitcast(F32), 0.0).then_inc(zeros_set, 1)
            for k in range(SLOTS - 2):
                nc.gpsimd.memset(xt[:, k, CG * QB * WP:], 0.0).then_inc(zeros_set, 1)
            nc.gpsimd.memset(per_hi[:, :, :].bitcast(F32), 0.0).then_inc(zeros_set, 1)
            nc.gpsimd.memset(per_lo[:, :, :].bitcast(F32), 0.0).then_inc(zeros_set, 1)

            def rest_of_periods(g):
                if not isinstance(g, int) or g >= 1:
                    pool.wait_ge(band_lo_made, g * CG)
                    pool.wait_ge(lo_made, (g * SLOTS - 1) * PAIRS + AHEAD)
                for q in range(QR):
                    if q > 0:
                        pool.wait_ge(per_lo_made, g * QR + q)
                    pool.wait_ge(per_hi_made, g * QR + q + 1)
                    part, at = slice(q * BLK, (q + 1) * BLK), slice(q * PERIOD, q * PERIOD + NJ)
                    nc.gpsimd.tensor_tensor(per_lo[part, :, at], periods_g[part, g],
                                            per_hi[part, :, at].bitcast(F32), ALU.subtract)\
                        .then_inc(per_lo_made, 1)

            def band_lo(g, c):
                pool.wait_ge(per_lo_made, g * QR + QR)
                nc.gpsimd.tensor_tensor(bands_of(c, 1), mask_of(), repeated(per_lo[:, c, :].bitcast(F32)),
                                        ALU.mult).then_inc(band_lo_made, 1)

            def rest(n, slot):
                pool.wait_ge(hi_made, n + 1)
                nc.gpsimd.tensor_tensor(lo[:, slot % RING], patches[:, slot % 2],
                                        hi[:, slot % RING].bitcast(F32), ALU.subtract).then_inc(lo_made, 1)

            def quads(g, first, last):
                for k in range(SLOTS):
                    t = g * SLOTS + k
                    if k == SLOTS - 1 and not last:
                        rest_of_periods(g + 1)
                        pool.wait_ge(per_lo_made, (g + 2) * QR)
                    for p in range(PAIRS):
                        n, slot = t * PAIRS + p + AHEAD, k * PAIRS + p + AHEAD
                        if not (last and slot >= SLOTS * PAIRS):
                            rest(n, slot)
                        if k == SLOTS - 1 and not last and p > 0:
                            pool.wait_ge(conv_made, t * CG + 2 * p)
                            band_lo(g + 1, 2 * p - 2)
                            band_lo(g + 1, 2 * p - 1)
                        if k == 0 and p == 0 and not first:
                            pool.wait_ge(conv_made, t * CG)
                            band_lo(g, CG - 2)
                            band_lo(g, CG - 1)

            pool.wait_ge(consts_in, 48)
            pool.wait_ge(period_made, NJ)
            for k in range(SLOTS - 2, SLOTS):
                nc.gpsimd.memset(xt[:, k, CG * QB * WP:], 0.0).then_inc(zeros_set, 1)
            pool.wait_ge(zeros_set, SLOTS + 3)
            rest_of_periods(0)
            band_lo(0, 0)
            band_lo(0, 1)
            rest(0, 0)
            for c in range(2, CG):
                band_lo(0, c)
            for n in range(1, AHEAD):
                rest(n, n)
            quads(0, True, False)
            with pool.Fori(1, G - 1) as g:
                quads(g, False, False)
            quads(G - 1, False, True)

        @block.vector
        def _(dve):
            def scale_of(t, k, step):
                if step == "inverse":
                    dve.wait_ge(root_made, t * 2 + 2)
                    nc.vector.reciprocal(inverse[:, :], root[:, :]).then_inc(scale_step, 1)
                if step == "square":
                    dve.wait_ge(scale_step, after(t, "inverse"))
                    nc.vector.scalar_tensor_tensor(out=square[:, :], in0=inverse[:, :], scalar=-0.5, in1=inverse[:, :],
                                                   op0=ALU.mult, op1=ALU.mult).then_inc(scale_step, 1)
                if step == "ratio":
                    dve.wait_ge(scale_step, after(t, "square"))
                    nc.vector.tensor_tensor(ratio[:, :], square[:, :], var[:, :], ALU.mult).then_inc(scale_step, 1)
                if step == "scale":
                    dve.wait_ge(scale_step, after(t, "ratio"))
                    nc.vector.scalar_tensor_tensor(out=scale[:, k % SLOTS, :], in0=ratio[:, :], scalar=1.5,
                                                   in1=inverse[:, :], op0=ALU.add, op1=ALU.mult)\
                        .then_inc(scale_step, 1)

            def to_patches(n, slot, quad):
                k, c = slot // PAIRS % SLOTS, slot % PAIRS * 2
                if not isinstance(n, int) or n >= 2:
                    dve.wait_ge(lo_made, n - 1)
                dve.wait_ge(border_set, quad * 2 + 2)
                first = xt[:, k, c * WP:c * WP + 1]
                src = bass.AP(tensor=first.tensor, offset=first.offset,
                              ap=[first.ap[0], [CG * WP, QB], [OUTW, 2 * NBLK], [1, BLK]])
                nc.vector.transpose(patches[:, slot % 2, :, 1:1 + BLK], src).then_inc(patches_made, 1)

            def from_patches(t, k, c, first):
                dve.wait_ge(conv_made, t * CG + c + 1)
                if c == 0 and not (first and k == 0):
                    dve.wait_ge(added, (t * 2 - 1) * QB)
                if c == CG // 2 and not (first and k == 0):
                    dve.wait_ge(added, t * 2 * QB)
                at = c % (CG // 2) * NBLK
                dst = z[:, c // (CG // 2), :, at:at + NBLK, :]
                nc.vector.transpose(dst, conv[:, c % BANKS, :, 0:HALF]).then_inc(bank_free, 1)

            def add(t, k, half, b):
                if half == 0 and b == 0:
                    dve.wait_ge(scale_step, after(t, "scale"))
                dve.wait_ge(bank_free, t * CG + (half + 1) * (CG // 2) + BANKS)
                at = (b * CG + half * (CG // 2)) * WP + HALO
                result = xt[:, k, at:at + CG // 2 * WP].rearrange("p (n w) -> p n w", w=OUTW)
                nc.vector.scalar_tensor_tensor(out=result, in0=z[:, half, b, :, 0:OUTW], scalar=scale[:, k, b:b + 1],
                                               in1=result, op0=ALU.mult, op1=ALU.add).then_inc(added, 1)

            def band_hi(g, c):
                dve.wait_ge(per_hi_made, g * QR + QR)
                nc.vector.tensor_tensor(bands_of(c, 0), mask_of(), repeated(per_hi[:, c, :].bitcast(F32)), ALU.mult)\
                    .then_inc(band_hi_made, 1)

            def quads(g, first, last):
                for k in range(SLOTS):
                    t = g * SLOTS + k
                    for c in range(CG):
                        if c % 2 == 0 and not (last and k * PAIRS + c // 2 + AHEAD >= SLOTS * PAIRS):
                            to_patches(t * PAIRS + c // 2 + AHEAD, k * PAIRS + c // 2 + AHEAD,
                                       t + (c // 2 + AHEAD) // PAIRS)
                        from_patches(t, k, c, first)
                        if c == 3:
                            scale_of(t, k, "square")
                        if k == SLOTS - 1 and not last:
                            band_hi(g + 1, c)
                        if c % 2 == 1:
                            for b in (c % (CG // 2) - 1, c % (CG // 2)):
                                if c >= CG // 2:
                                    add(t, k, 0, b)
                                elif not (first and k == 0):
                                    add(t - 1, (k - 1) % SLOTS, 1, b)
                        if c == 2:
                            scale_of(t, k, "inverse")
                        if c == 3:
                            scale_of(t, k, "ratio")
                        if c == 4:
                            scale_of(t, k, "scale")
                if last:
                    for b in range(QB):
                        add(t, k, 1, b)

            nc.vector.memset(ones[:, :], 1.0).then_inc(ones_set, 1)
            nc.vector.memset(eps[:, :], EPS).then_inc(ones_set, 1)
            dve.wait_ge(consts_in, 48)
            for j in range(NJ):
                dve.wait_ge(period_made, j + 1)
                nc.vector.tensor_copy(periods[:, :, j], conv[:, j // 2 % BANKS, j % 2, 0:C]).then_inc(period_kept, 1)
            dve.wait_ge(zeros_set, SLOTS + 3)
            for c in range(CG):
                band_hi(0, c)
            for n in range(AHEAD):
                to_patches(n, n, 0)
            dve.sem_inc(bank_free, BANKS)
            quads(0, True, False)
            with dve.Fori(1, G - 1) as g:
                quads(g, False, False)
            quads(G - 1, False, True)


def tap_selection():
    s = np.zeros((TAPS, DH, PERIOD, QR, BLK), np.float32)
    for d in range(DH):
        for r in range(PERIOD):
            for wi in range(BLK):
                at = 5 * (DH - 1 - d) + (wi - r) % PERIOD
                if at in POS:
                    s[POS.index(at), d, r, :, wi] = 1.0
                if at in NEG:
                    s[NEG.index(at), d, r, :, wi] = -1.0
    return s.reshape(TAPS, DH * PERIOD, P)


def band_positions():
    m = np.zeros((QR, BLK, -(-OUTW // PERIOD) * PERIOD), np.float32)
    for wi in range(BLK):
        m[:, wi, max(0, wi - 2 * HALO):min(OUTW, wi + 1)] = 1.0
    return m.reshape(P, -1)


def kernel(x, L0_conv_weight):
    import numpy as _np
    import concourse.bacc as _bacc
    from concourse import mybir as _mybir
    from concourse.bass_utils import run_bass_kernel_spmd as _run

    nc = _bacc.Bacc("TRN2", target_bir_lowering=False, num_devices=1)
    arrays = {
        "x_dram": _np.ascontiguousarray(x),
        "taps_dram": _np.ascontiguousarray(_np.asarray(L0_conv_weight).reshape(-1, TAPS + 1)[:, 1:].T),
        "tap_select_dram": tap_selection(),
        "band_mask_dram": band_positions(),
    }
    args = [nc.dram_tensor(n, a.shape, _mybir.dt.from_np(a.dtype), kind="ExternalInput").ap()
            for n, a in arrays.items()]
    out = nc.dram_tensor("out_dram", arrays["x_dram"].shape, _mybir.dt.float32, kind="ExternalOutput").ap()
    preact_conv(nc, *args, out)
    r = _run(nc, [arrays], core_ids=[0])
    return r.results[0]["out_dram"]
```
